# Optimizing a Trainium2 kernel written in Bass

```python
import numpy as np
import jax
import jax.numpy as jnp

def _softmax(x, axis=-1):
    return jax.nn.softmax(x, axis=axis)

def _gelu(x):
    return jax.nn.gelu(x, approximate=True)

def _silu(x):
    return jax.nn.silu(x)

def _sigmoid(x):
    return jax.nn.sigmoid(x)

def _layernorm(x, axis=-1, eps=1e-05):
    m = jnp.mean(x, axis=axis, keepdims=True)
    v = jnp.var(x, axis=axis, keepdims=True)
    return (x - m) / jnp.sqrt(v + eps)

def _scatter_add(tgt, idx, src, axis=0):
    return tgt.at[idx].add(src)

def _segment_sum(src, seg, n):
    return jax.ops.segment_sum(src, seg, n)
kernel_name = 'mk_xattn_seq_d2_seqx_r8_492f7a'

def setup_inputs(seed: int=0):
    np.random.seed(seed)
    _w = jnp.asarray

    def _rec_inputs():
        import jax
        import jax.numpy as jnp
        _rk = jax.random.key(seed)
        x = -0.0003929 + 0.9999 * jax.random.normal(jax.random.fold_in(_rk, 1), (4, 256, 512), jnp.float32)
        _lenS = 256 - jax.random.randint(jax.random.fold_in(_rk, 7), (4,), 0, max(1, 256 // 4) + 1, jnp.int32)
        _lenS2 = 1601 - jax.random.randint(jax.random.fold_in(_rk, 8), (4,), 0, max(1, 1601 // 4) + 1, jnp.int32)
        _ctx_4096P = jax.random.normal(jax.random.fold_in(_rk, 11), (4, 16, 512), jnp.float32)
        _ctx_4096c = jax.random.dirichlet(jax.random.fold_in(_rk, 511), 0.3 * jnp.ones((16,), jnp.float32), (4, 1601))
        _ctx_4096t = jnp.einsum('bsk,bkd->bsd', _ctx_4096c, _ctx_4096P)
        _ctx_4096t = _ctx_4096t * jax.lax.rsqrt(jnp.mean(jnp.square(_ctx_4096t)) + 1e-12) * 0.953939
        ctx_4096 = 2.81802e-05 + 1.00001 * (_ctx_4096t + 0.3 * jax.random.normal(jax.random.fold_in(_rk, 611), (4, 1601, 512), jnp.float32))
        _validS = jnp.arange(256)[None, :] < _lenS[:, None]
        _validS2 = jnp.arange(1601)[None, :] < _lenS2[:, None]
        _causal = jnp.tril(jnp.ones((256, 256), dtype=bool))
        mask_BxS2_ik0 = jnp.where(jnp.broadcast_to(_validS2[:, :], (4, 1601)), 0, 1).astype(jnp.int32)
        return (x, ctx_4096, mask_BxS2_ik0)
    x, ctx_4096, mask_BxS2_ik0 = _rec_inputs()

    def _L0_xattn_setup():
        import jax, jax.numpy as jnp
        import numpy as np
        H = 512
        NH = 32
        NKV = 8
        HD = H // NH
        R = 16
        SCALING = 32.0 / 16.0

        def _lora_linear(x, W, A, B):
            return x @ W + SCALING * (x @ A @ B)
        key = jax.random.key(seed)
        ks = jax.random.split(key, 16)
        d = {'hidden_states': jax.random.normal(ks[0], (4, 128, H), jnp.float32), 'traces': jax.random.normal(ks[1], (4, 128, H), jnp.float32), 'Wq': jax.random.normal(ks[2], (H, H), jnp.float32) * 0.02, 'Aq': jax.random.normal(ks[3], (H, R), jnp.float32) * 0.02, 'Bq': jax.random.normal(ks[4], (R, H), jnp.float32) * 0.02, 'Wk': jax.random.normal(ks[5], (H, NKV * HD), jnp.float32) * 0.02, 'Ak': jax.random.normal(ks[6], (H, R), jnp.float32) * 0.02, 'Bk': jax.random.normal(ks[7], (R, NKV * HD), jnp.float32) * 0.02, 'Wv': jax.random.normal(ks[8], (H, NKV * HD), jnp.float32) * 0.02, 'Av': jax.random.normal(ks[9], (H, R), jnp.float32) * 0.02, 'Bv': jax.random.normal(ks[10], (R, NKV * HD), jnp.float32) * 0.02, 'Wo': jax.random.normal(ks[11], (H, H), jnp.float32) * 0.02, 'Ao': jax.random.normal(ks[12], (H, R), jnp.float32) * 0.02, 'Bo': jax.random.normal(ks[13], (R, H), jnp.float32) * 0.02}
        return d
    _L0_xattn_all = _L0_xattn_setup()
    _L0_xattn_in = {k: v for k, v in _L0_xattn_all.items() if k in ('Wq', 'Aq', 'Bq', 'Wk', 'Ak', 'Bk', 'Wv', 'Av', 'Bv', 'Wo', 'Ao', 'Bo')}
    del _L0_xattn_all

    def _L1_xattn_setup():
        import jax, jax.numpy as jnp
        import numpy as np
        H = 512
        NH = 32
        HD = H // NH
        key = jax.random.key(seed)
        ks = jax.random.split(key, 12)
        B, L, V = (2, 128, 128)
        s = 1.0 / np.sqrt(H)
        return {'hidden_states': jax.random.normal(ks[0], (B, L, H), jnp.float32), 'vision_features': jax.random.normal(ks[1], (B, V, H), jnp.float32), 'attention_mask': jax.random.randint(ks[2], (B, V), 0, 2, jnp.int32), 'Wq': jax.random.normal(ks[3], (H, H), jnp.float32) * s, 'bq': jnp.zeros((H,), jnp.float32), 'Wk': jax.random.normal(ks[4], (H, H), jnp.float32) * s, 'bk': jnp.zeros((H,), jnp.float32), 'Wv': jax.random.normal(ks[5], (H, H), jnp.float32) * s, 'bv': jnp.zeros((H,), jnp.float32), 'Wo': jax.random.normal(ks[6], (H, H), jnp.float32) * s, 'bo': jnp.zeros((H,), jnp.float32), 'ln_g': jnp.ones((H,), jnp.float32), 'ln_b': jnp.zeros((H,), jnp.float32)}
    _L1_xattn_all = _L1_xattn_setup()
    _L1_xattn_in = {k: v for k, v in _L1_xattn_all.items() if k in ('Wq', 'bq', 'Wk', 'bk', 'Wv', 'bv', 'Wo', 'bo', 'ln_g', 'ln_b')}
    del _L1_xattn_all
    return {'x': x, 'ctx_4096': ctx_4096, 'mask_BxS2_ik0': mask_BxS2_ik0, 'L0_xattn_Wq': _L0_xattn_in['Wq'], 'L0_xattn_Aq': _L0_xattn_in['Aq'], 'L0_xattn_Bq': _L0_xattn_in['Bq'], 'L0_xattn_Wk': _L0_xattn_in['Wk'], 'L0_xattn_Ak': _L0_xattn_in['Ak'], 'L0_xattn_Bk': _L0_xattn_in['Bk'], 'L0_xattn_Wv': _L0_xattn_in['Wv'], 'L0_xattn_Av': _L0_xattn_in['Av'], 'L0_xattn_Bv': _L0_xattn_in['Bv'], 'L0_xattn_Wo': _L0_xattn_in['Wo'], 'L0_xattn_Ao': _L0_xattn_in['Ao'], 'L0_xattn_Bo': _L0_xattn_in['Bo'], 'L1_xattn_Wq': _L1_xattn_in['Wq'], 'L1_xattn_bq': _L1_xattn_in['bq'], 'L1_xattn_Wk': _L1_xattn_in['Wk'], 'L1_xattn_bk': _L1_xattn_in['bk'], 'L1_xattn_Wv': _L1_xattn_in['Wv'], 'L1_xattn_bv': _L1_xattn_in['bv'], 'L1_xattn_Wo': _L1_xattn_in['Wo'], 'L1_xattn_bo': _L1_xattn_in['bo'], 'L1_xattn_ln_g': _L1_xattn_in['ln_g'], 'L1_xattn_ln_b': _L1_xattn_in['ln_b']}

def reference(x, ctx_4096, mask_BxS2_ik0, L0_xattn_Wq, L0_xattn_Aq, L0_xattn_Bq, L0_xattn_Wk, L0_xattn_Ak, L0_xattn_Bk, L0_xattn_Wv, L0_xattn_Av, L0_xattn_Bv, L0_xattn_Wo, L0_xattn_Ao, L0_xattn_Bo, L1_xattn_Wq, L1_xattn_bq, L1_xattn_Wk, L1_xattn_bk, L1_xattn_Wv, L1_xattn_bv, L1_xattn_Wo, L1_xattn_bo, L1_xattn_ln_g, L1_xattn_ln_b):
    import jax
    import jax.numpy as jnp

    def _L0_xattn_ref(hidden_states, traces, Wq, Aq, Bq, Wk, Ak, Bk, Wv, Av, Bv, Wo, Ao, Bo):
        import jax, jax.numpy as jnp
        import numpy as np
        H = 512
        NH = 32
        NKV = 8
        HD = H // NH
        R = 16
        SCALING = 32.0 / 16.0

        def _lora_linear(x, W, A, B):
            return x @ W + SCALING * (x @ A @ B)
        bsz, q_len, _ = hidden_states.shape
        t_len = traces.shape[1]
        groups = NH // NKV
        q = _lora_linear(hidden_states, Wq, Aq, Bq).reshape(bsz, q_len, NH, HD)
        q = jnp.transpose(q, (0, 2, 1, 3))
        k = _lora_linear(traces, Wk, Ak, Bk).reshape(bsz, t_len, NKV, HD)
        v = _lora_linear(traces, Wv, Av, Bv).reshape(bsz, t_len, NKV, HD)
        k = jnp.transpose(k, (0, 2, 1, 3))
        v = jnp.transpose(v, (0, 2, 1, 3))
        k = jnp.repeat(k, groups, axis=1)
        v = jnp.repeat(v, groups, axis=1)
        scores = jnp.einsum('bhqd,bhtd->bhqt', q, k) / jnp.sqrt(jnp.asarray(HD, q.dtype))
        attn = jax.nn.softmax(scores, axis=-1)
        context = jnp.einsum('bhqt,bhtd->bhqd', attn, v)
        context = jnp.transpose(context, (0, 2, 1, 3)).reshape(bsz, q_len, H)
        out = _lora_linear(context, Wo, Ao, Bo)
        return hidden_states + out

    def _L1_xattn_ref(hidden_states, vision_features, attention_mask, Wq, bq, Wk, bk, Wv, bv, Wo, bo, ln_g, ln_b):
        import jax, jax.numpy as jnp
        import numpy as np
        H = 512
        NH = 32
        HD = H // NH
        B, L, _ = hidden_states.shape
        Vn = vision_features.shape[1]
        Q = (hidden_states @ Wq.T + bq).reshape(B, L, NH, HD)
        K = (vision_features @ Wk.T + bk).reshape(B, Vn, NH, HD)
        Vv = (vision_features @ Wv.T + bv).reshape(B, Vn, NH, HD)
        scores = jnp.einsum('blhd,bvhd->bhlv', Q, K) / np.sqrt(HD).astype(np.float32)
        mask = (attention_mask != 0)[:, None, None, :]
        scores = jnp.where(mask, scores, -jnp.inf)
        attn = jax.nn.softmax(scores, axis=-1)
        ctx = jnp.einsum('bhlv,bvhd->blhd', attn, Vv).reshape(B, L, H)
        attn_out = ctx @ Wo.T + bo
        x = hidden_states + attn_out
        mu = jnp.mean(x, axis=-1, keepdims=True)
        var = jnp.mean(jnp.square(x - mu), axis=-1, keepdims=True)
        return (x - mu) / jnp.sqrt(var + 1e-05) * ln_g + ln_b
    x = _L0_xattn_ref(x, ctx_4096, L0_xattn_Wq, L0_xattn_Aq, L0_xattn_Bq, L0_xattn_Wk, L0_xattn_Ak, L0_xattn_Bk, L0_xattn_Wv, L0_xattn_Av, L0_xattn_Bv, L0_xattn_Wo, L0_xattn_Ao, L0_xattn_Bo)
    x = _L1_xattn_ref(x, ctx_4096, mask_BxS2_ik0, L1_xattn_Wq, L1_xattn_bq, L1_xattn_Wk, L1_xattn_bk, L1_xattn_Wv, L1_xattn_bv, L1_xattn_Wo, L1_xattn_bo, L1_xattn_ln_g, L1_xattn_ln_b)
    return x

_drawn_inputs = setup_inputs


def setup_inputs(seed=0):
    import zlib

    import numpy as np

    out = dict(_drawn_inputs(seed))
    spreads = {'L1_xattn_bq': (0.0, 0.422),
     'L1_xattn_bk': (0.0, 0.8),
     'L1_xattn_bv': (0.0, 0.1),
     'L1_xattn_bo': (0.0, 0.1),
     'L1_xattn_ln_g': (1.0, 0.2),
     'L1_xattn_ln_b': (0.0, 0.1)}
    factors = {'L0_xattn_Wq': 8.0,
     'L0_xattn_Aq': 8.0,
     'L0_xattn_Bq': 8.0,
     'L0_xattn_Wk': 8.0,
     'L0_xattn_Ak': 8.0,
     'L0_xattn_Bk': 8.0,
     'L0_xattn_Av': 3.667,
     'L0_xattn_Bv': 3.395,
     'L0_xattn_Ao': 3.808,
     'L0_xattn_Bo': 3.964}
    for name, (base, spread) in spreads.items():
        noise = np.random.default_rng([zlib.crc32(name.encode()), seed]).standard_normal(out[name].shape)
        drawn = base * np.exp(spread * noise) if base else spread * noise
        out[name] = jnp.asarray(drawn.astype(out[name].dtype))
    for name, factor in factors.items():
        out[name] = (out[name] * factor).astype(out[name].dtype)
    return out
```

```python
import concourse.bass as bass
import concourse.mybir as mybir
from concourse.alu_op_type import AluOpType as ALU
from contextlib import ExitStack

F32, BF16, I32 = mybir.dt.float32, mybir.dt.bfloat16, mybir.dt.int32
ACT = mybir.ActivationFunctionType
AX = mybir.AxisListType


class Signal:

    def __init__(self, sem):
        self.sem, self.value = sem, 0

    def next(self, by=1):
        self.value += by
        return self.value


class Queue:

    def __init__(self):
        self.steps, self.reached = [], {}

    def wait(self, mark):
        if mark is None:
            return
        signal, value = mark
        if value > self.reached.get(signal, 0):
            self.reached[signal] = value
            self.steps.append(lambda e: e.wait_ge(signal.sem, value))

    def do(self, make, signal=None, by=1):
        if signal is None:
            self.steps.append(make)
            return None
        self.steps.append(lambda e: make(e).then_inc(signal.sem, by))
        return signal, signal.next(by)

    def play(self, engine):
        for step in self.steps:
            step(engine)


def cross_attention_pair(nc, x, xT, ctxT, mask, w0, w1, out):
    B, S, H = x.shape
    T = ctxT.shape[2]
    P = 128
    HD = 16
    NH = H // HD
    NKV = w0["Wk"].shape[1] // HD
    RANK = w0["AqT"].shape[0]
    LORA = 32.0 / RANK
    KT = H // P
    QT = S // P
    GH = 4
    UB = NH // GH
    L0 = B * UB
    UNITS = 2 * L0
    TT = 124
    NT = -(-T // TT)
    CT = 4
    CW = CT * TT
    NC = -(-T // CW)
    MW = -(-T // 4)
    NM = -(-T // MW)
    ROWS = QT * GH
    CHUNKS = ROWS * NM
    KPARTS = (0, 0, 0, 1, 1, 2)
    QPARTS = (0, 1, 2, 0, 1, 0)
    MROW = 6 * HD
    KMAX, KEXP = MROW + 1, MROW + 3
    VW = HD + 1
    VCOLS = 8 * VW + 15
    NEG = -1.0e30
    SCALE = HD ** -0.5
    EPS = 1e-5
    LEAD = 10
    LAG = 2

    def tile(i):
        return i * TT, min(TT, T - i * TT)

    ctx = ExitStack()
    with ctx:
        def sb(name, shape, dt=F32):
            return ctx.enter_context(nc.sbuf_tensor(name, shape, dt))

        def sig(name):
            return Signal(ctx.enter_context(nc.semaphore(name)))

        ctx_sb = sb("ctx_sb", [P, KT, T])
        k_stack = sb("k_stack", [KEXP, 12, T], BF16)
        k_parts = sb("k_parts", [P, 3, T], BF16)
        full = sb("full", [P, 2, CW])
        rest = sb("rest", [P, 2, CW])
        v_sb = sb("v_sb", [P, 2, NT, VCOLS])
        p_sb = sb("p_sb", [P, 6, 512])
        wq = sb("wq", [P, KT, H])
        wo = sb("wo", [P, KT, H])
        wk0 = sb("wk0", [P, KT, NKV * HD])
        wv0 = sb("wv0", [P, KT, NKV * HD])
        wk1 = sb("wk1", [P, KT, H])
        wv1 = sb("wv1", [P, KT, H])
        x_sb = sb("x_sb", [P, B * QT, H])
        xt_sb = sb("xt_sb", [P, 2, KT, S])
        q_parts = sb("q_parts", [P, 2, 3, S], BF16)
        q_stack = sb("q_stack", [KEXP, 4, GH, S], BF16)
        o_sb = sb("o_sb", [P, 2, S])
        att = sb("att", [P, QT, H])
        att_t = sb("att_t", [P, KT, S])
        row_bias = sb("row_bias", [P, 4, H])
        col_bias = sb("col_bias", [P, 2, KT])
        ident = sb("ident", [P, P])
        valid_rows = sb("valid_rows", [NT, B, TT])
        valid = sb("valid", [TT, B, NT])
        neg_row = sb("neg_row", [B, T], BF16)
        chunk_max = sb("chunk_max", [P, 2, ROWS, NM])
        neg_max = sb("neg_max", [P, 2, ROWS])
        max_parts = sb("max_parts", [ROWS, 2, 2, P], BF16)
        recip = sb("recip", [P, 2, QT, GH])
        stats = sb("stats", [P, QT, 6])
        moments = sb("moments", [P, QT, 2])
        rstd = sb("rstd", [P, QT])
        lora_a = att_t[0:RANK, :, :].rearrange("p k s -> p (k s)")
        lora_b = att[0:RANK, :, :].rearrange("p q h -> p (q h)")
        mask_rows = p_sb[0:B, 0:4, :].rearrange("p a n -> p (a n)")[:, 0:T].bitcast(I32)
        mask_tiles = p_sb[0:NT, 4:6, :].rearrange("p a n -> p (a n)")[:, 0:B * TT].bitcast(I32)\
            .rearrange("p (b t) -> p b t", b=B)

        score_bank = [ctx.enter_context(nc.psum_tensor(f"score{i}", [P, 512], F32)) for i in range(3)]
        max_bank = [ctx.enter_context(nc.psum_tensor(f"max{i}", [P, 512], F32)) for i in range(2)]
        value_bank = ctx.enter_context(nc.psum_tensor("value", [P, 512], F32))
        work_bank = [ctx.enter_context(nc.psum_tensor(f"work{i}", [P, 512], F32)) for i in range(2)]

        s_const = sig("s_const")
        s_scores = sig("s_scores")
        s_exp = sig("s_exp")
        s_rows = sig("s_rows")
        s_chunk = sig("s_chunk")
        s_value = sig("s_value")
        s_work = sig("s_work")
        s_act = sig("s_act")
        s_dve = sig("s_dve")
        s_split = sig("s_split")
        s_ones = sig("s_ones")
        s_w = {n: sig(f"s_w_{n}") for n in ("lora_a", "lora_b", "wq", "wk0", "wv0", "wo", "wk1", "wv1",
                                            "wq1", "wo1", "rows", "cols", "mask", "x")}
        s_ctx = [sig(f"s_ctx{c}") for c in range(NC)]
        s_xt = [sig(f"s_xt{i}") for i in range(2)]
        s_kst = [sig(f"s_kst{i}") for i in range(3)]
        s_qst = [sig(f"s_qst{i}") for i in range(4)]
        s_mst = [sig(f"s_mst{i}") for i in range(4)]
        s_out = sig("s_out")

        pe, act, dve, pool, sp = Queue(), Queue(), Queue(), Queue(), Queue()

        def load(dst, src, signal):
            return sp.do(lambda e: e.dma_start(dst, src), signal, 16)

        work_free = [None, None]
        work_turn = [0]

        later = []
        filling = [False]

        def work():
            assert not filling[0]
            n = work_turn[0] % 2
            work_turn[0] += 1
            for entry in [x for x in later if x[0] == n]:
                later.remove(entry)
                entry[1]()
            pe.wait(work_free[n])
            return n, work_bank[n]

        def flush():
            while later:
                later.pop(0)[1]()

        def const(make):
            mark = pool.do(make, s_const)
            pool.wait(mark)
            return mark

        const(lambda e: e.memset(ident[:, :], 0.0))
        ident_done = const(lambda e: e.affine_select(
            out=ident[:, :], in_=ident[:, :], compare_op=ALU.not_equal, fill=1.0, base=0,
            pattern=[[-1, P]], channel_multiplier=1))
        tiles_zero = dve.do(lambda e: e.memset(mask_tiles, 0), s_dve)
        const(lambda e: e.memset(q_stack[MROW:KEXP, :, :, :], 1.0))
        for g in range(3):
            const(lambda e, g=g: e.memset(k_stack[MROW:KEXP, 4 * g:4 * g + 4, :], 1.0))
            stack_ones = const(lambda e, g=g: e.memset(k_stack[MROW:KMAX, 4 * g:4 * g + 4, :], 0.0))
        for s in range(2):
            const(lambda e, s=s: e.memset(v_sb[:, s, :, 8 * VW:VCOLS], 0.0))
            v_const = const(lambda e, s=s: e.memset(v_sb[:, s, :, HD:8 * VW:VW], 1.0))

        def by_tile(w):
            return w.rearrange("(k p) n -> p k n", p=P)

        ctx_loaded = [None] * NC
        ctx_read = [None] * NC

        def load_ctx(b, c):
            lo, hi = c * CW, min(T, (c + 1) * CW)
            sp.wait(ctx_read[c])
            ctx_loaded[c] = load(ctx_sb[:, :, lo:hi], ctxT[b].rearrange("(k p) t -> p k t", p=P)[:, :, lo:hi],
                                 s_ctx[c])

        xt_ready = [None, None]
        xt_read = [None, None]

        def load_xt(b):
            s = b % 2
            sp.wait(xt_read[s])
            xt_ready[s] = load(xt_sb[:, s, :, :], xT[b].rearrange("(k p) s -> p k s", p=P), s_xt[s])

        offsets, widths = {}, {"k": NKV * HD, "v": NKV * HD, "q": H, "o": H}
        a_loaded = {}
        weights = {"k": (wk0, "Wk", "wk0"), "q": (wq, "Wq", "wq"), "v": (wv0, "Wv", "wv0"), "o": (wo, "Wo", "wo")}
        w_loaded, w_ready = {}, {}

        def load_w(name, dst, src):
            w_loaded[name] = load(dst[:, :, :], by_tile(src), s_w[name])

        lora_read = [None]

        def load_lora(n):
            sp.wait(lora_read[0])
            a = load(lora_a[:, 0:H], w0[f"A{n}T"], s_w["lora_a"])
            b = load(lora_b[:, 0:widths[n]], w0[f"B{n}"], s_w["lora_b"])
            a_loaded[n] = (a, b)

        def fold_lora(n):
            dst, _, name = weights[n]
            for mark in (*a_loaded[n], w_loaded[name]):
                pe.wait(mark)
                dve.wait(mark)
            for k in range(KT):
                i, bank = work()
                full_mark = pe.do(lambda e, k=k, bank=bank: e.matmul(
                    bank[:, 0:widths[n]], lora_a[:, k * P:(k + 1) * P], lora_b[:, 0:widths[n]],
                    start=True, stop=True), s_work)
                dve.wait(full_mark)
                work_free[i] = dve.do(lambda e, k=k, bank=bank: e.scalar_tensor_tensor(
                    out=dst[:, k, :], in0=bank[:, 0:widths[n]], scalar=LORA, in1=dst[:, k, :],
                    op0=ALU.mult, op1=ALU.add), s_dve)
                w_ready[name] = work_free[i]
            lora_read[0] = full_mark

        load_lora("k")
        load_w("wk0", wk0, w0["Wk"])
        load_ctx(0, 0)
        load_w("wq", wq, w0["Wq"])
        for c in range(1, NC):
            load_ctx(0, c)
        load_xt(0)
        load_w("wv0", wv0, w0["Wv"])
        sp.wait(tiles_zero)
        for b in range(B):
            load(mask_rows[b:b + 1, :], mask[b:b + 1, :], s_w["mask"])
            load(mask_tiles[0:NT - 1, b, :], mask[b, 0:(NT - 1) * TT].rearrange("(i t) -> i t", t=TT),
                 s_w["mask"])
            mask_loaded = load(mask_tiles[NT - 1:NT, b, 0:T - (NT - 1) * TT], mask[b:b + 1, (NT - 1) * TT:T],
                               s_w["mask"])

        dve.wait(mask_loaded)
        neg_done = dve.do(lambda e: e.tensor_scalar(neg_row[:, :], mask_rows, 0.0, NEG, ALU.is_equal,
                                                    ALU.mult), s_dve)
        valid_done = dve.do(lambda e: e.tensor_scalar(valid_rows[:, :, :], mask_tiles, 0.0, None,
                                                      ALU.not_equal), s_dve)
        p_free = [valid_done] * 6

        def turn_mask():
            i, bank = work()
            pe.wait(valid_done)
            pe.wait(ident_done)
            for b in range(B):
                mark = pe.do(lambda e, b=b: e.transpose(bank[0:TT, b * NT:(b + 1) * NT], valid_rows[:, b, :],
                                                        ident[0:NT, 0:NT]), s_work)
            dve.wait(mark)
            work_free[i] = dve.do(lambda e: e.tensor_copy(
                valid[:, :, :], bank[0:TT, 0:B * NT].rearrange("p (b i) -> p b i", b=B)), s_dve)
            return work_free[i]

        full_free = [None, None]
        split_turn = [0]

        def split(mark, bank, i, n, dst, bias, dst_free, done):
            s = split_turn[0] % 2
            split_turn[0] += 1
            act.wait(mark)
            act.wait(full_free[s])
            for m in dst_free:
                act.wait(m)
            act.do(lambda e: e.activation(full[:, s, 0:n], bank[:, 0:n], ACT.Identity, bias=bias), s_act)
            work_free[i] = act.do(lambda e: e.activation(dst[:, 0, :], bank[:, 0:n], ACT.Identity,
                                                         bias=bias), s_act)
            pool.wait(work_free[i])
            for m in dst_free:
                pool.wait(m)
            pool.do(lambda e: e.tensor_tensor(rest[:, s, 0:n], full[:, s, 0:n], dst[:, 0, :], ALU.subtract),
                    s_split)
            mid = pool.do(lambda e: e.tensor_tensor(dst[:, 1, :], full[:, s, 0:n], dst[:, 0, :],
                                                    ALU.subtract), s_split)
            pool.wait(mid)
            full_free[s] = pool.do(lambda e: e.tensor_tensor(dst[:, 2, :], rest[:, s, 0:n], dst[:, 1, :],
                                                             ALU.subtract), s_split)
            done(full_free[s])

        k_parts_ready = [None]
        k_parts_read = [None]
        v_ready = [None, None]
        v_read = [None, None]
        q_parts_ready = [None, None]
        q_parts_read = [None, None]

        def product(box, lhs, rhs, m, n, k, first_waits=(), off=0):
            if k == 0:
                box["i"], box["bank"] = work()
            filling[0] = k < KT - 1
            for mark in first_waits:
                pe.wait(mark)
            bank = box["bank"]
            make = lambda e: e.matmul(bank[0:m, off:off + n], lhs, rhs, start=(k == 0), stop=(k == KT - 1))
            return pe.do(make, s_work if k == KT - 1 else None)

        def k_tasks(layer, col):
            w = wk1 if layer else wk0
            tasks = []
            for c in range(NC):
                lo, hi = c * CW, min(T, (c + 1) * CW)
                box = {}
                for k in range(KT):
                    def task(c=c, k=k, lo=lo, hi=hi, box=box):
                        mark = product(box, w[:, k, col * P:(col + 1) * P], ctx_sb[:, k, lo:hi], P, hi - lo, k,
                                       (ctx_loaded[c], w_loaded["wk1"] if layer else w_ready["wk0"]))
                        if k == KT - 1:
                            ctx_read[c] = mark
                            bias = col_bias[:, 1, col:col + 1] if layer else 0.0

                            def reader():
                                if layer:
                                    act.wait(w_loaded["cols"])
                                split(mark, box["bank"], box["i"], hi - lo, k_parts[:, :, lo:hi], bias,
                                      (k_parts_read[0],), lambda m: k_parts_ready.__setitem__(0, m))
                            later.append((box["i"], reader))
                    tasks.append(task)
            return tasks

        def q_tasks(layer, b, pair):
            tasks = []
            box, slot = {}, pair % 2
            for k in range(KT):
                def task(k=k):
                    mark = product(box, wq[:, k, pair % (UB // 2) * P:(pair % (UB // 2) + 1) * P],
                                   xt_sb[:, b % 2, k, :], P, S, k,
                                   (xt_ready[b % 2], w_loaded["wq1"] if layer else w_ready["wq"]))
                    if k == KT - 1:
                        xt_read[b % 2] = mark
                        col = pair % (UB // 2)
                        bias = col_bias[:, 0, col:col + 1] if layer else 0.0

                        def reader():
                            if layer:
                                act.wait(w_loaded["cols"])
                            split(mark, box["bank"], box["i"], S, q_parts[:, slot, :, :], bias,
                                  (q_parts_read[slot],), lambda m: q_parts_ready.__setitem__(slot, m))
                        later.append((box["i"], reader))
                tasks.append(task)
            return tasks

        def v_tasks(layer, b, col, slot):
            w = wv1 if layer else wv0
            tasks = []
            if layer:
                def ones_task():
                    pool.wait(v_read[slot])
                    pool.wait(valid_t)
                    pool.wait(v_const)
                    ones = pool.do(lambda e: e.tensor_copy(
                        v_sb[0:TT, slot, :, HD:8 * VW:VW],
                        valid[:, b, :].rearrange("p (i o) -> p i o", o=1).broadcast_to([TT, NT, 8])), s_ones)
                    v_ones[slot] = ones
                tasks.append(ones_task)
            for i in range(NT):
                t0, tn = tile(i)
                c = i // CT
                box = {}
                for k in range(KT):
                    def task(i=i, k=k, t0=t0, tn=tn, c=c, box=box):
                        mark = product(box, ctx_sb[:, k, t0:t0 + tn], w[:, k, col * P:(col + 1) * P], tn, P, k,
                                       (ctx_loaded[c], w_loaded["wv1"] if layer else w_ready["wv0"]))
                        if k == KT - 1:
                            ctx_read[c] = mark

                            def reader():
                                act.wait(mark)
                                act.wait(v_read[slot])
                                act.wait(v_const)
                                dst = v_sb[0:tn, slot, i, 0:8 * VW].rearrange("p (h e) -> p h e", e=VW)
                                src = box["bank"][0:tn, 0:P].rearrange("p (h d) -> p h d", d=HD)
                                if layer:
                                    act.wait(valid_t)
                                    make = lambda e: e.activation(dst[:, :, 0:HD], src, ACT.Copy,
                                                                  scale=valid[0:tn, b, i:i + 1])
                                else:
                                    make = lambda e: e.activation(dst[:, :, 0:HD], src, ACT.Copy)
                                work_free[box["i"]] = v_ready[slot] = act.do(make, s_act)
                            later.append((box["i"], reader))
                    tasks.append(task)
            return tasks

        v_ones = [v_const, v_const]
        x_ready = [None] * (B * QT)

        def turn_x_tasks(b):
            tasks = []
            for q in range(QT):
                def task(q=q):
                    i, bank = work()
                    pe.wait(x_ready[b * QT + q])
                    for k in range(KT):
                        mark = pe.do(lambda e, k=k: e.transpose(
                            bank[:, k * P:(k + 1) * P], x_sb[:, b * QT + q, k * P:(k + 1) * P], ident[:, :]),
                            s_work if k == KT - 1 else None)

                    def reader():
                        act.wait(mark)
                        act.wait(xt_read[b % 2])
                        work_free[i] = xt_ready[b % 2] = act.do(lambda e: e.activation(
                            xt_sb[:, b % 2, :, q * P:(q + 1) * P],
                            bank[:, :].rearrange("p (k s) -> p k s", k=KT), ACT.Copy), s_act)
                    later.append((i, reader))
                tasks.append(task)
            return tasks

        k_slot_ready = [None] * 3
        k_slot_read = [None] * 3
        q_slot_ready = [None] * 4
        q_slot_read = [None] * 4
        m_slot_ready = [None] * 4
        m_unit = [None] * 4

        def k_place(u):
            if u < L0:
                return (u // 4) % 3, u % 4
            return (L0 // 4 + u - L0) % 3, 0

        def stack(u):
            g, _ = k_place(u)
            if u >= L0 or u % 4 == 0:
                half = 64 * (u % 2 if u >= L0 else (u // 4) % 2)
                sp.wait(k_parts_ready[0])
                sp.wait(stack_ones)
                for mark in k_slot_read[g] or ():
                    sp.wait(mark)
                for r, part in enumerate(KPARTS):
                    for h in range(4):
                        mark = load(k_stack[r * HD:(r + 1) * HD, 4 * g + h, :],
                                    k_parts[half + h * HD:half + (h + 1) * HD, part, :], s_kst[g])
                k_parts_read[0] = mark
                if u >= L0:
                    b = (u - L0) // UB
                    sp.wait(neg_done)
                    for h in range(4):
                        mark = load(k_stack[MROW:KMAX, 4 * g + h, :], neg_row[b:b + 1, :], s_kst[g])
                    k_parts_read[0] = mark
                k_slot_ready[g] = mark
            s, pair = u % 4, u // 2
            sp.wait(q_parts_ready[pair % 2])
            for mark in q_slot_read[s] or ():
                sp.wait(mark)
            for r, part in enumerate(QPARTS):
                for h in range(4):
                    row = 64 * (u % 2) + h * HD
                    mark = load(q_stack[r * HD:(r + 1) * HD, s, h, :],
                                q_parts[row:row + HD, pair % 2, part, :], s_qst[s])
            q_parts_read[pair % 2] = q_slot_ready[s] = mark

        max_free = [None, None]
        neg_max_read = [None, None]
        max_parts_read = [None, None]
        max_turn = [0]

        def max_chunk():
            n = max_turn[0]
            u, at = n // CHUNKS, n % CHUNKS
            if u >= UNITS:
                return
            max_turn[0] += 1
            row, c = at // NM, at % NM
            q, h = row // GH, row % GH
            g, first = k_place(u)
            head = 4 * g + (first if u < L0 else h)
            lo, hi = c * MW, min(T, (c + 1) * MW)
            pe.wait(max_free[n % 2])
            pe.wait(k_slot_ready[g])
            pe.wait(q_slot_ready[u % 4])
            bank = max_bank[n % 2]
            mark = pe.do(lambda e: e.matmul(bank[:, 0:hi - lo], q_stack[0:KMAX, u % 4, h, q * P:(q + 1) * P],
                                            k_stack[0:KMAX, head, lo:hi], start=True, stop=True), s_rows)
            dve.wait(mark)
            if at == 0:
                dve.wait(neg_max_read[u % 2])
            max_free[n % 2] = dve.do(lambda e: e.tensor_reduce(
                chunk_max[:, u % 2, row, c:c + 1], bank[:, 0:hi - lo], AX.X, ALU.max), s_chunk)
            if at == CHUNKS - 1:
                dve.wait(max_free[n % 2])
                neg = dve.do(lambda e: e.tensor_reduce(neg_max[:, u % 2, :], chunk_max[:, u % 2, :, :], AX.X,
                                                       ALU.max, negate=True), s_dve)
                turns.append(lambda: max_rows(u, neg))

        turns = []

        def turn_all():
            while turns and not filling[0]:
                turns.pop(0)()

        def max_rows(u, neg):
            i, bank = work()
            pe.wait(neg)
            pe.wait(ident_done)
            mark = pe.do(lambda e: e.transpose(bank[0:ROWS, 0:P], neg_max[:, u % 2, :], ident[:, :]), s_work)
            neg_max_read[u % 2] = mark

            def reader():
                dve.wait(mark)
                dve.wait(max_parts_read[u % 2])
                high = dve.do(lambda e: e.tensor_copy(max_parts[:, u % 2, 0, :], bank[0:ROWS, 0:P]), s_dve)
                dve.wait(high)
                work_free[i] = dve.do(lambda e: e.tensor_tensor(
                    max_parts[:, u % 2, 1, :], bank[0:ROWS, 0:P], max_parts[:, u % 2, 0, :], ALU.subtract),
                    s_dve)
                sp.wait(work_free[i])
                for m in q_slot_read[u % 4] or ():
                    sp.wait(m)
                for q in range(QT):
                    for part in range(2):
                        m = load(q_stack[KMAX + part:KMAX + part + 1, u % 4, :, q * P:(q + 1) * P],
                                 max_parts[q * GH:(q + 1) * GH, u % 2, part, :], s_mst[u % 4])
                m_slot_ready[u % 4] = max_parts_read[u % 2] = m
                m_unit[u % 4] = u
            later.append((i, reader))

        score_free = [None] * 3
        half_turn = [0]
        value_free = [None]
        exp_done = {}

        def scores(u, i, half):
            n = half_turn[0]
            half_turn[0] += 1
            t0, tn = tile(i)
            g, first = k_place(u)
            s = u % 4
            bank, place = score_bank[n % 3], n % 6
            assert m_unit[s] == u, (u, i, m_unit, max_turn, len(turns), len(later))
            pe.wait(score_free[n % 3])
            pe.wait(k_slot_ready[g])
            pe.wait(q_slot_ready[s])
            pe.wait(m_slot_ready[s])
            if u < L0:
                mark = pe.do(lambda e: e.matmul(
                    bank[0:tn, :], k_stack[0:KEXP, 4 * g + first, t0:t0 + tn],
                    q_stack[0:KEXP, s, 2 * half:2 * half + 2, :].rearrange("p h q -> p (h q)"),
                    start=True, stop=True), s_scores)
            else:
                for j in range(2):
                    h = 2 * half + j
                    mark = pe.do(lambda e, j=j, h=h: e.matmul(
                        bank[0:tn, j * S:(j + 1) * S], k_stack[0:KEXP, 4 * g + h, t0:t0 + tn],
                        q_stack[0:KEXP, s, h, :], start=True, stop=True), s_scores if j else None)
            if i == NT - 1 and half == 1:
                q_slot_read[s] = (mark,)
                if u >= L0 or u % 4 == 3:
                    k_slot_read[g] = (mark, )
            act.wait(mark)
            act.wait(p_free[place])
            score_free[n % 3] = act.do(lambda e: e.activation(
                p_sb[0:tn, place, :], bank[0:tn, :], ACT.Exp, scale=SCALE), s_exp)
            exp_done[u, i, half] = score_free[n % 3], place

        def values(u, i):
            t0, tn = tile(i)
            slot = (u // UB) % 2 if u < L0 else ((u - L0) // 2) % 2
            if i == 0:
                pe.wait(value_free[0])
                pe.wait(v_ready[slot])
                pe.wait(v_ones[slot])
            places = []
            for half in range(2):
                mark, place = exp_done.pop((u, i, half))
                pe.wait(mark)
                places.append(place)
            for j in range(GH):
                head = u % UB if u < L0 else 4 * (u % 2) + j
                done = pe.do(lambda e, j=j, head=head: e.matmul(
                    value_bank[32 * j:32 * j + 32, 0:S], v_sb[0:tn, slot, i, head * VW:head * VW + 32],
                    p_sb[0:tn, places[j // 2], j % 2 * S:(j % 2 + 1) * S], start=(i == 0),
                    stop=(i == NT - 1)), s_value if j == GH - 1 else None)
            for place in places:
                p_free[place] = done
            if i == NT - 1:
                v_read[slot] = done
                finish(u, done)

        o_read = [None, None]
        recip_turn = [0]
        att_ready = [None]
        att_read = [None]

        def finish(u, done):
            s = u % 2
            dve.wait(done)
            dve.wait(o_read[s])
            value_free[0] = dve.do(lambda e: e.tensor_copy(o_sb[:, s, :], value_bank[:, 0:S]), s_dve)
            copied = value_free[0]
            h0 = GH * (u % UB)

            def turn():
                i, bank = work()
                pe.wait(copied)
                for q in range(QT):
                    mark = pe.do(lambda e, q=q: e.transpose(bank[:, q * P:(q + 1) * P],
                                                            o_sb[:, s, q * P:(q + 1) * P], ident[:, :]), s_work)
                o_read[s] = mark
                view = bank[:, 0:QT * P].rearrange("p (q h e) -> p q h e", q=QT, h=GH)

                def reader():
                    dve.wait(mark)
                    dve.wait(att_read[0])
                    inv = dve.do(lambda e: e.reciprocal(recip[:, s, :, :], view[:, :, :, HD]), s_dve)
                    dve.wait(inv)
                    for q in range(QT):
                        m = dve.do(lambda e, q=q: e.tensor_tensor(
                            att[:, q, h0 * HD:(h0 + GH) * HD].rearrange("p (h d) -> p h d", h=GH),
                            view[:, q, :, 0:HD],
                            recip[:, s, q, :].rearrange("p (h o) -> p h o", o=1).broadcast_to([P, GH, HD]),
                            ALU.mult), s_dve)
                    work_free[i] = att_ready[0] = m
                later.append((i, reader))
            turns.append(turn)

        att_t_ready = [None] * QT
        att_t_read = [None]

        def out_tasks(layer, b):
            tasks = []
            ready = [None]

            def first():
                ready[0] = att_ready[0]
                if layer:
                    dve.wait(att_ready[0])
                    dve.wait(w_loaded["rows"])
                    for q in range(QT):
                        ready[0] = dve.do(lambda e, q=q: e.tensor_tensor(
                            att[:, q, :], att[:, q, :], row_bias[:, 0, :], ALU.add), s_dve)
            tasks.append(first)
            for q in range(QT):
                def task(q=q):
                    i, bank = work()
                    pe.wait(ready[0])
                    for k in range(KT):
                        mark = pe.do(lambda e, k=k: e.transpose(
                            bank[:, k * P:(k + 1) * P], att[:, q, k * P:(k + 1) * P], ident[:, :]),
                            s_work if k == KT - 1 else None)
                    att_read[0] = mark

                    def reader():
                        act.wait(mark)
                        act.wait(att_t_read[0])
                        work_free[i] = att_t_ready[q] = act.do(lambda e: e.activation(
                            att_t[:, :, q * P:(q + 1) * P], bank[:, :].rearrange("p (k s) -> p k s", k=KT),
                            ACT.Copy), s_act)
                    later.append((i, reader))
                tasks.append(task)
            for q in range(QT):
                box = {}
                for k in range(KT):
                    def task(q=q, k=k, box=box):
                        mark = product(box, att_t[:, k, q * P:(q + 1) * P], wo[:, k, :], P, H, k,
                                       (att_t_ready[q], w_loaded["wo1"] if layer else w_ready["wo"]))
                        if k < KT - 1:
                            return
                        wo_read[0] = mark
                        if q == QT - 1:
                            att_t_read[0] = mark
                        later.append((box["i"], lambda: (norm if layer else add)(b, q, mark, box)))
                    tasks.append(task)
            return tasks

        wo_read = [None]

        def add(b, q, mark, box):
            row, bank = b * QT + q, box["bank"]
            dve.wait(mark)
            dve.wait(x_loaded)
            work_free[box["i"]] = x_ready[row] = dve.do(lambda e: e.tensor_tensor(
                x_sb[:, row, :], bank[:, :], x_sb[:, row, :], ALU.add), s_dve)

        def norm(b, q, mark, box):
            row, bank = b * QT + q, box["bank"]
            y = x_sb[:, row, :]

            def step(make):
                m = dve.do(make, s_dve)
                dve.wait(m)
                return m
            dve.wait(mark)
            dve.wait(x_ready[row])
            work_free[box["i"]] = step(lambda e: e.tensor_tensor(y, bank[:, :], y, ALU.add))
            step(lambda e: e.tensor_tensor(y, y, row_bias[:, 1, :], ALU.add))
            step(lambda e: e.bn_stats(stats[:, q, :], y))
            step(lambda e: e.bn_aggr(moments[:, q, :], stats[:, q, :]))
            m = step(lambda e: e.tensor_scalar(rstd[:, q:q + 1], moments[:, q, 1:2], EPS, None, ALU.add))
            act.wait(m)
            root = act.do(lambda e: e.activation(rstd[:, q:q + 1], rstd[:, q:q + 1], ACT.Sqrt), s_act)
            dve.wait(root)
            step(lambda e: e.reciprocal(rstd[:, q:q + 1], rstd[:, q:q + 1]))
            step(lambda e: e.tensor_scalar(y, y, moments[:, q, 0:1], rstd[:, q:q + 1], ALU.subtract, ALU.mult))
            step(lambda e: e.tensor_tensor(y, y, row_bias[:, 2, :], ALU.mult))
            m = step(lambda e: e.tensor_tensor(y, y, row_bias[:, 3, :], ALU.add))
            sp.wait(m)
            load(out[b, q * P:(q + 1) * P, :], y, s_out)

        def run(tasks):
            for t in tasks:
                t()
            flush()

        fold_lora("k")
        run(k_tasks(0, 0))
        load_lora("q")
        fold_lora("q")
        run(q_tasks(0, 0, 0))
        stack(0)
        run(q_tasks(0, 0, 1))
        stack(1)
        load_lora("v")
        fold_lora("v")
        valid_t = turn_mask()
        load_w("wo", wo, w0["Wo"])
        load_lora("o")
        load_w("wk1", wk1, w1["Wk"])
        load_w("wv1", wv1, w1["Wv"])
        x_loaded = load(x_sb[:, :, :], x.rearrange("b (q p) h -> p (b q) h", p=P), s_w["x"])
        for n, v in enumerate(("bv", "bo", "ln_g", "ln_b")):
            w_loaded["rows"] = load(row_bias[:, n, :], w1[v].rearrange("(o n) -> o n", o=1)
                                    .broadcast_to([P, H]), s_w["rows"])
        for n, v in enumerate(("bq", "bk")):
            w_loaded["cols"] = load(col_bias[:, n, :], w1[v], s_w["cols"])
        v0 = v_tasks(0, 0, 0, 0)
        for n in range(CHUNKS + LEAD):
            max_chunk()
            if n < len(v0):
                v0[n]()
            turn_all()
        flush()
        for t in v0[CHUNKS + LEAD:]:
            t()
        fold_lora("o")
        flush()

        def after_value(u):
            tasks = []
            if u % UB == 0 and u > 0:
                b = u // UB - 1
                tasks += out_tasks(b // B, b % B)
            v = u + 2
            if v % 2 == 0 and L0 <= v < UNITS:
                b = (v - L0) // UB
                vt = v_tasks(1, b, v % UB // 2, v // 2 % 2)
                tasks += vt
                if v % UB == UB - 2 and b + 1 < B:
                    for c in range(NC):
                        tasks.append(lambda c=c: load_ctx(b + 1, c))
            return tasks

        def window(u):
            tasks = []
            if u == L0 + 1:
                def task():
                    sp.wait(wo_read[0])
                    load_w("wo1", wo, w1["Wo"])
                tasks.append(task)
            if u < L0 - UB:
                b = u // UB + 1
                at = u % UB
                vt, kt = v_tasks(0, b, 0, b % 2), k_tasks(0, 0)
                if at == 0:
                    for c in range(NC):
                        tasks.append(lambda c=c: load_ctx(b, c))
                    tasks.append(lambda: load_xt(b))
                if at < 3:
                    n = KT * -(-len(vt) // (3 * KT))
                    tasks += v_parts.setdefault(b, vt)[at * n:(at + 1) * n]
                elif at < 6:
                    n = KT * -(-len(kt) // (3 * KT))
                    tasks += kq_parts.setdefault(b, kt)[(at - 3) * n:(at - 2) * n]
            if u == L0 - 6:
                for c in range(NC):
                    tasks.append(lambda c=c: load_ctx(0, c))
            v = u + 3
            if v % 2 == 0 and 4 <= v < UNITS:
                layer, b = v // L0, v % L0 // UB
                if layer:
                    tasks += k_tasks(1, v % UB // 2)
                tasks += q_tasks(layer, b, v // 2)
                if v == L0 - 2:
                    def task():
                        sp.wait(xt_read[(B - 1) % 2])
                        load_w("wq1", wq, w1["Wq"])
                    tasks.append(task)
            if u + 4 >= L0 and (u + 4) % UB == 0 and u + 4 < UNITS:
                tasks += turn_x_tasks((u + 4 - L0) // UB)
            return tasks

        v_parts, kq_parts = {}, {}
        waiting = []
        for u in range(UNITS):
            if u + 2 < UNITS:
                stack(u + 2)
            tasks = window(u)
            ran = 0
            base = max_turn[0]
            for i in range(NT):
                if i == LAG:
                    while filling[0]:
                        tasks[ran]()
                        ran += 1
                    tasks[ran:ran] = after_value(u)
                goal = base + CHUNKS * (i + 1) // NT
                scores(u, i, 0)
                flush()
                if max_turn[0] < goal:
                    max_chunk()
                scores(u, i, 1)
                upto = max(ran, ran + (len(tasks) - ran) // (NT - i))
                mid = (ran + upto + 1) // 2
                while ran < mid:
                    tasks[ran]()
                    ran += 1
                    turn_all()
                if max_turn[0] < goal and max_turn[0] < UNITS * CHUNKS:
                    max_chunk()
                waiting.append((u, i))
                if len(waiting) > LAG:
                    values(*waiting.pop(0))
                while ran < upto:
                    tasks[ran]()
                    ran += 1
                    turn_all()
                while max_turn[0] < goal and max_turn[0] < UNITS * CHUNKS:
                    max_chunk()
                while turns:
                    if filling[0]:
                        tasks[ran]()
                        ran += 1
                    turn_all()
                flush()
        while waiting:
            values(*waiting.pop(0))
        turn_all()
        flush()
        run(out_tasks(1, B - 1))
        sp.wait((s_out, s_out.value))

        block = ctx.enter_context(nc.Block())
        block.sync(lambda e: sp.play(e))
        block.tensor(lambda e: pe.play(e))
        block.scalar(lambda e: act.play(e))
        block.vector(lambda e: dve.play(e))
        block.gpsimd(lambda e: pool.play(e))


def kernel(**inputs):
    import numpy as np
    import concourse.bacc as bacc
    from concourse.bass_utils import run_bass_kernel_spmd

    a = {k: np.asarray(v) for k, v in inputs.items()}
    H = a["x"].shape[2]
    arrays = {
        "x": a["x"],
        "xT": a["x"].transpose(0, 2, 1),
        "ctxT": a["ctx_4096"].transpose(0, 2, 1),
        "mask": a["mask_BxS2_ik0"],
    }
    for n in "qkvo":
        arrays[f"l0_W{n}"] = a[f"L0_xattn_W{n}"]
        arrays[f"l0_A{n}T"] = a[f"L0_xattn_A{n}"].T
        arrays[f"l0_B{n}"] = a[f"L0_xattn_B{n}"]
        arrays[f"l1_W{n}"] = a[f"L1_xattn_W{n}"].T
    for n in ("bq", "bk"):
        arrays[f"l1_{n}"] = a[f"L1_xattn_{n}"].reshape(H // 128, 128).T
    for n in ("bv", "bo", "ln_g", "ln_b"):
        arrays[f"l1_{n}"] = a[f"L1_xattn_{n}"]
    arrays = {k: np.ascontiguousarray(v) for k, v in arrays.items()}

    nc = bacc.Bacc("TRN2", target_bir_lowering=False, num_devices=1)
    t = {k: nc.dram_tensor(k, v.shape, mybir.dt.from_np(v.dtype), kind="ExternalInput").ap()
         for k, v in arrays.items()}
    out = nc.dram_tensor("out", a["x"].shape, F32, kind="ExternalOutput").ap()
    w0 = {k[3:]: v for k, v in t.items() if k.startswith("l0_")}
    w1 = {k[3:]: v for k, v in t.items() if k.startswith("l1_")}
    cross_attention_pair(nc, t["x"], t["xT"], t["ctxT"], t["mask"], w0, w1, out)
    return run_bass_kernel_spmd(nc, [arrays], core_ids=[0]).results[0]["out"]
```

```python
import concourse.bass as bass
import concourse.mybir as mybir
from concourse.alu_op_type import AluOpType as ALU
from contextlib import ExitStack

F32, BF16, I32 = mybir.dt.float32, mybir.dt.bfloat16, mybir.dt.int32
ACT = mybir.ActivationFunctionType
AX = mybir.AxisListType


class Signal:

    def __init__(self, sem):
        self.sem, self.value = sem, 0

    def next(self, by=1):
        self.value += by
        return self.value


class Queue:

    def __init__(self):
        self.steps, self.reached = [], {}

    def wait(self, mark):
        if mark is None:
            return
        signal, value = mark
        if value > self.reached.get(signal, 0):
            self.reached[signal] = value
            self.steps.append(lambda e: e.wait_ge(signal.sem, value))

    def do(self, make, signal=None, by=1):
        if signal is None:
            self.steps.append(make)
            return None
        self.steps.append(lambda e: make(e).then_inc(signal.sem, by))
        return signal, signal.next(by)

    def play(self, engine):
        for step in self.steps:
            step(engine)


def cross_attention_pair(nc, x, xT, ctxT, mask, w0, w1, out):
    B, S, H = x.shape
    T = ctxT.shape[2]
    P = 128
    HD = 16
    NH = H // HD
    NKV = w0["Wk"].shape[1] // HD
    RANK = w0["AqT"].shape[0]
    LORA = 32.0 / RANK
    KT = H // P
    QT = S // P
    GH = 4
    UB = NH // GH
    L0 = B * UB
    UNITS = 2 * L0
    TT = 124
    NT = -(-T // TT)
    CT = 4
    CW = CT * TT
    NC = -(-T // CW)
    MW = -(-T // 4)
    NM = -(-T // MW)
    QROWS = QT * 8
    ROWS = QT * GH
    CHUNKS = ROWS * NM
    KPARTS = (0, 1, 2, 0, 1, 0)
    MROW = 6 * HD
    KMAX, KEXP = MROW + 1, MROW + 3
    VW = HD + 1
    VCOLS = 8 * VW + 15
    NEG = -1.0e30
    SCALE = HD ** -0.5
    EPS = 1e-5
    LEAD = 12
    LAG = 3
    PLACES = 2 * (LAG + 1)

    def tile(i):
        return i * TT, min(TT, T - i * TT)

    ctx = ExitStack()
    with ctx:
        def sb(name, shape, dt=F32):
            return ctx.enter_context(nc.sbuf_tensor(name, shape, dt))

        def sig(name):
            return Signal(ctx.enter_context(nc.semaphore(name)))

        ctx_sb = sb("ctx_sb", [P, KT, T])
        k_flat = sb("k_flat", [KEXP, 12 * T], BF16)
        k_stack = k_flat[:, :].rearrange("p (h t) -> p h t", t=T)
        k_parts = sb("k_parts", [P, 2, 3, CW], BF16)
        full = sb("full", [P, 2, CW])
        rest = sb("rest", [P, CW])
        v_sb = sb("v_sb", [P, 2, NT, VCOLS])
        p_sb = sb("p_sb", [P, PLACES, 512])
        wq = sb("wq", [P, KT, H])
        wo = sb("wo", [P, KT, H])
        wk0 = sb("wk0", [P, KT, NKV * HD])
        wv0 = sb("wv0", [P, KT, NKV * HD])
        wk1 = sb("wk1", [P, KT, H])
        wv1 = sb("wv1", [P, KT, H])
        x_sb = sb("x_sb", [P, B * QT, H])
        xt_sb = sb("xt_sb", [P, 2, KT, S])
        q_nat = sb("q_nat", [P, 2, QT * 8, MROW], BF16)
        q_stack = sb("q_stack", [KEXP, 3, GH, S], BF16)
        m_nat = sb("m_nat", [P, 2, ROWS, 32], BF16)
        o_sb = sb("o_sb", [P, 2, S])
        att = sb("att", [P, QT, H])
        att_t = sb("att_t", [P, KT, S])
        row_bias = sb("row_bias", [P, 5, H])
        col_bias = sb("col_bias", [P, KT])
        k_dram = nc.dram_tensor("k_dram", [2, 3, P, T], BF16, kind="Internal").ap()
        ident = sb("ident", [P, P])
        ident16 = sb("ident16", [P, P], BF16)
        valid_rows = sb("valid_rows", [NT, B, TT])
        valid = sb("valid", [TT, B, NT])
        neg_row = sb("neg_row", [B, T], BF16)
        chunk_max = sb("chunk_max", [P, 2, ROWS, NM])
        neg_max = sb("neg_max", [P, 2, ROWS])
        recip = sb("recip", [P, 2, QT, GH])
        stats = sb("stats", [P, QT, 6])
        moments = sb("moments", [P, QT, 2])
        rstd = sb("rstd", [P, QT])
        lora_a = att_t[0:RANK, :, :].rearrange("p k s -> p (k s)")
        lora_b = att[0:RANK, :, :].rearrange("p q h -> p (q h)")
        mask_rows = p_sb[0:B, 0:4, :].rearrange("p a n -> p (a n)")[:, 0:T].bitcast(I32)
        mask_tiles = p_sb[0:NT, 4:6, :].rearrange("p a n -> p (a n)")[:, 0:B * TT].bitcast(I32)\
            .rearrange("p (b t) -> p b t", b=B)

        score_bank = [ctx.enter_context(nc.psum_tensor(f"score{i}", [P, 512], F32)) for i in range(2)]
        max_bank = [ctx.enter_context(nc.psum_tensor(f"max{i}", [P, 512], F32)) for i in range(3)]
        value_bank = ctx.enter_context(nc.psum_tensor("value", [P, 512], F32))
        work_bank = [ctx.enter_context(nc.psum_tensor(f"work{i}", [P, 512], F32)) for i in range(2)]

        work_bank16 = [bank[:, :].bitcast(BF16) for bank in work_bank]

        s_const = sig("s_const")
        s_scores = sig("s_scores")
        s_exp = sig("s_exp")
        s_rows = sig("s_rows")
        s_chunk = sig("s_chunk")
        s_value = sig("s_value")
        s_work = sig("s_work")
        s_act = sig("s_act")
        s_dve = sig("s_dve")
        s_split = sig("s_split")
        s_ones = sig("s_ones")
        s_w = {n: sig(f"s_w_{n}") for n in ("lora_a0", "lora_b0", "lora_a1", "lora_b1", "wq", "wk0", "wv0", "wo", "wk1", "wv1",
                                            "wq1", "wo1", "rows", "cols", "mask", "x")}
        s_ctx = [sig(f"s_ctx{c}") for c in range(NC)]
        s_xt = [sig(f"s_xt{i}") for i in range(2)]
        s_kdw = [sig(f"s_kdw{i}") for i in range(2)]
        s_kst = [sig(f"s_kst{i}") for i in range(3)]
        s_out = sig("s_out")

        pe, act, dve, pool, sp = Queue(), Queue(), Queue(), Queue(), Queue()

        def load(dst, src, signal):
            return sp.do(lambda e: e.dma_start(dst, src), signal, 16)

        work_free = [None, None]
        work_turn = [0]

        later = []
        filling = [False]

        def work():
            assert not filling[0]
            n = work_turn[0] % 2
            work_turn[0] += 1
            for entry in [x for x in later if x[0] == n]:
                later.remove(entry)
                entry[1]()
            pe.wait(work_free[n])
            return n, work_bank[n]

        def work16():
            n, _ = work()
            return n, work_bank16[n]

        def flush():
            while later:
                later.pop(0)[1]()

        def const(make):
            mark = pool.do(make, s_const)
            pool.wait(mark)
            return mark

        const(lambda e: e.memset(ident[:, :], 0.0))
        ident_done = const(lambda e: e.affine_select(
            out=ident[:, :], in_=ident[:, :], compare_op=ALU.not_equal, fill=1.0, base=0,
            pattern=[[-1, P]], channel_multiplier=1))
        const(lambda e: e.memset(q_stack[MROW:KEXP, :, :, :], 1.0))
        const(lambda e: e.memset(m_nat[:, :, :, :], 0.0))
        m_const = const(lambda e: e.memset(m_nat[:, :, :, 0:1], 1.0))
        ident16_done = const(lambda e: e.tensor_copy(ident16[:, :], ident[:, :]))
        for s in range(2):
            const(lambda e, s=s: e.memset(v_sb[:, s, :, 8 * VW:VCOLS], 0.0))
            v_const = const(lambda e, s=s: e.memset(v_sb[:, s, :, HD:8 * VW:VW], 1.0))

        stack_ones = [None] * 3

        def constant_rows(g, queue, signal):
            rows = k_stack[:, 4 * g:4 * (g + 1), :]
            queue.wait((signal, signal.value))
            ones = queue.do(lambda e: e.memset(rows[MROW:KEXP, :, :], 1.0), signal)
            queue.wait(ones)
            stack_ones[g] = queue.do(lambda e: e.memset(rows[MROW:KMAX, :, :], 0.0), signal)

        def by_tile(w):
            return w.rearrange("(k p) n -> p k n", p=P)

        ctx_loaded = [None] * NC
        ctx_read = [None] * NC

        def load_ctx(b, c):
            lo, hi = c * CW, min(T, (c + 1) * CW)
            sp.wait(ctx_read[c])
            ctx_loaded[c] = load(ctx_sb[:, :, lo:hi], ctxT[b].rearrange("(k p) t -> p k t", p=P)[:, :, lo:hi],
                                 s_ctx[c])

        xt_ready = [None, None]
        xt_read = [None, None]

        def load_xt(b):
            s = b % 2
            sp.wait(xt_read[s])
            xt_ready[s] = load(xt_sb[:, s, :, :], xT[b].rearrange("(k p) s -> p k s", p=P), s_xt[s])

        widths = {"k": NKV * HD, "v": NKV * HD, "q": H, "o": H}
        a_loaded = {}
        weights = {"k": (wk0, "Wk", "wk0"), "q": (wq, "Wq", "wq"), "v": (wv0, "Wv", "wv0"), "o": (wo, "Wo", "wo")}
        w_loaded, w_ready = {}, {}

        def load_w(name, dst, src):
            w_loaded[name] = load(dst[:, :, :], by_tile(src), s_w[name])

        lora_read = [None, None]
        lora_slot = {"k": 0, "q": 1, "v": 0, "o": 1}

        def load_lora(n):
            s = lora_slot[n]
            sp.wait(lora_read[s])
            a = load(lora_a[:, s * H:(s + 1) * H], w0[f"A{n}T"], s_w[f"lora_a{s}"])
            b = load(lora_b[:, s * H:s * H + widths[n]], w0[f"B{n}"], s_w[f"lora_b{s}"])
            a_loaded[n] = (a, b)

        def fold_lora(n):
            dst, _, name = weights[n]
            s = lora_slot[n]
            for mark in (*a_loaded[n], w_loaded[name]):
                pe.wait(mark)
                dve.wait(mark)
            for k in range(KT):
                i, bank = work()
                full_mark = pe.do(lambda e, k=k, bank=bank: e.matmul(
                    bank[:, 0:widths[n]], lora_a[:, s * H + k * P:s * H + (k + 1) * P],
                    lora_b[:, s * H:s * H + widths[n]],
                    start=True, stop=True), s_work)
                dve.wait(full_mark)
                work_free[i] = dve.do(lambda e, k=k, bank=bank: e.scalar_tensor_tensor(
                    out=dst[:, k, :], in0=bank[:, 0:widths[n]], scalar=LORA, in1=dst[:, k, :],
                    op0=ALU.mult, op1=ALU.add), s_dve)
                w_ready[name] = work_free[i]
            lora_read[s] = full_mark

        load_lora("k")
        load_w("wk0", wk0, w0["Wk"])
        load_ctx(0, 0)
        load_lora("q")
        load_w("wq", wq, w0["Wq"])
        load_xt(0)
        for c in range(1, NC):
            load_ctx(0, c)
        load_w("wv0", wv0, w0["Wv"])

        tiles_zero = dve.do(lambda e: e.memset(mask_tiles, 0), s_dve)
        sp.wait(tiles_zero)
        for b in range(B):
            load(mask_rows[b:b + 1, :], mask[b:b + 1, :], s_w["mask"])
            load(mask_tiles[0:NT - 1, b, :], mask[b, 0:(NT - 1) * TT].rearrange("(i t) -> i t", t=TT),
                 s_w["mask"])
            mask_loaded = load(mask_tiles[NT - 1:NT, b, 0:T - (NT - 1) * TT], mask[b:b + 1, (NT - 1) * TT:T],
                               s_w["mask"])
        masks = {}

        def read_mask():
            dve.wait(mask_loaded)
            masks["neg"] = dve.do(lambda e: e.tensor_scalar(neg_row[:, :], mask_rows, 0.0, NEG, ALU.is_equal,
                                                            ALU.mult), s_dve)
            masks["rows"] = dve.do(lambda e: e.tensor_scalar(valid_rows[:, :, :], mask_tiles, 0.0, None,
                                                             ALU.not_equal), s_dve)
            for n in range(PLACES):
                p_free[n] = masks["rows"]

        p_free = [None] * PLACES

        def turn_mask():
            i, bank = work()
            pe.wait(masks["rows"])
            pe.wait(ident_done)
            for b in range(B):
                mark = pe.do(lambda e, b=b: e.transpose(bank[0:TT, b * NT:(b + 1) * NT], valid_rows[:, b, :],
                                                        ident[0:NT, 0:NT]), s_work)
            dve.wait(mark)
            work_free[i] = dve.do(lambda e: e.tensor_copy(
                valid[:, :, :], bank[0:TT, 0:B * NT].rearrange("p (b i) -> p b i", b=B)), s_dve)
            return work_free[i]

        full_free = [None, None]
        split_turn = [0]

        def split(mark, bank, i, n, dst, bias, dst_free):
            s = split_turn[0] % 2
            split_turn[0] += 1
            act.wait(mark)
            act.wait(full_free[s])
            work_free[i] = act.do(lambda e: e.activation(full[:, s, 0:n], bank[:, 0:n], ACT.Identity,
                                                         bias=bias), s_act)
            pool.wait(work_free[i])
            pool.wait(dst_free)
            pool.wait((s_split, s_split.value))
            high = pool.do(lambda e: e.tensor_copy(dst[:, 0, :], full[:, s, 0:n]), s_split)
            pool.wait(high)
            pool.do(lambda e: e.tensor_tensor(rest[:, 0:n], full[:, s, 0:n], dst[:, 0, :], ALU.subtract),
                    s_split)
            mid = pool.do(lambda e: e.tensor_tensor(dst[:, 1, :], full[:, s, 0:n], dst[:, 0, :],
                                                    ALU.subtract), s_split)
            pool.wait(mid)
            full_free[s] = pool.do(lambda e: e.tensor_tensor(dst[:, 2, :], rest[:, 0:n], dst[:, 1, :],
                                                             ALU.subtract), s_split)
            return full_free[s]

        part_turn = [0]
        k_parts_read = [None, None]
        k_dram_ready = [None, None]
        k_dram_read = [[], []]
        v_ready = [None, None]
        v_read = [None, None]
        q_nat_ready = [None, None]
        q_nat_read = [None, None]

        def product(box, lhs, rhs, m, n, k, first_waits=(), off=0):
            if k == 0:
                box["i"], box["bank"] = work()
            filling[0] = k < KT - 1
            for mark in first_waits:
                pe.wait(mark)
            bank = box["bank"]
            make = lambda e: e.matmul(bank[0:m, off:off + n], lhs, rhs, start=(k == 0), stop=(k == KT - 1))
            return pe.do(make, s_work if k == KT - 1 else None)

        def k_tasks(layer, col, group):
            w = wk1 if layer else wk0
            tasks = []
            for c in range(NC):
                lo, hi = c * CW, min(T, (c + 1) * CW)
                box = {}
                for k in range(KT):
                    def task(c=c, k=k, lo=lo, hi=hi, box=box):
                        mark = product(box, w[:, k, col * P:(col + 1) * P], ctx_sb[:, k, lo:hi], P, hi - lo, k,
                                       (ctx_loaded[c], w_loaded["wk1"] if layer else w_ready["wk0"]))
                        if k == KT - 1:
                            ctx_read[c] = mark
                            bias = col_bias[:, col:col + 1] if layer else 0.0

                            def reader():
                                if layer:
                                    act.wait(w_loaded["cols"])
                                s = part_turn[0] % 2
                                part_turn[0] += 1
                                parts = split(mark, box["bank"], box["i"], hi - lo, k_parts[:, s, :, 0:hi - lo],
                                              bias, k_parts_read[s])
                                sp.wait(parts)
                                for m in k_dram_read[group % 2]:
                                    sp.wait(m)
                                k_parts_read[s] = load(
                                    k_dram[group % 2, :, :, lo:hi].rearrange("a p t -> p a t"),
                                    k_parts[:, s, :, 0:hi - lo], s_kdw[s])
                                k_dram_ready[group % 2] = list(k_parts_read)
                            later.append((box["i"], reader))
                    tasks.append(task)
            return tasks

        def q_tasks(layer, b, pair):
            tasks = []
            box, slot, col = {}, pair % 2, pair % (UB // 2)
            for q in range(QT):
                for k in range(KT):
                    def task(q=q, k=k):
                        if q:
                            filling[0] = k < KT - 1
                            pe.wait(xt_ready[b % 2])
                        lhs, rhs = xt_sb[:, b % 2, k, q * P:(q + 1) * P], wq[:, k, col * P:(col + 1) * P]
                        if q == 0:
                            product(box, lhs, rhs, P, P, k,
                                    (xt_ready[b % 2], w_loaded["wq1"] if layer else w_ready["wq"]))
                            filling[0] = True
                            return
                        bank = box["bank"]
                        mark = pe.do(lambda e: e.matmul(bank[:, q * P:(q + 1) * P], lhs, rhs, start=(k == 0),
                                                        stop=(k == KT - 1)), s_work if k == KT - 1 else None)
                        if k == KT - 1:
                            xt_read[b % 2] = mark
                            later.append((box["i"], lambda: split_q(layer, mark, box, slot, col)))
                    tasks.append(task)
            return tasks

        def split_q(layer, mark, box, slot, col):
            s, bank = split_turn[0] % 2, box["bank"]
            split_turn[0] += 1
            dve.wait(mark)
            dve.wait(full_free[s])
            if layer:
                dve.wait(w_loaded["rows"])
                bias = row_bias[:, 4, col * P:(col + 1) * P].rearrange("p (o n) -> p o n", o=1)\
                    .broadcast_to([P, QT, P])
                make = lambda e: e.tensor_tensor(full[:, s, 0:S].rearrange("p (q n) -> p q n", q=QT),
                                                 bank[:, 0:S].rearrange("p (q n) -> p q n", q=QT), bias, ALU.add)
            else:
                make = lambda e: e.tensor_copy(full[:, s, 0:S], bank[:, 0:S])
            work_free[box["i"]] = dve.do(make, s_dve)
            one = full[:, s, 0:S].rearrange("p (n d) -> p n d", d=HD)
            left = rest[:, 0:S].rearrange("p (n d) -> p n d", d=HD)
            dst = q_nat[:, slot, :, :].rearrange("p n (r d) -> p n r d", d=HD)

            def times(v, r):
                return v.rearrange("p n (o d) -> p n o d", o=1).broadcast_to([P, QROWS, r, HD])
            pool.wait(work_free[box["i"]])
            pool.wait(q_nat_read[slot])
            pool.wait((s_split, s_split.value))
            high = pool.do(lambda e: e.tensor_copy(dst[:, :, 0:3, :], times(one, 3)), s_split)
            pool.wait(high)
            pool.do(lambda e: e.tensor_tensor(left, one, dst[:, :, 0, :], ALU.subtract), s_split)
            mid = pool.do(lambda e: e.tensor_tensor(dst[:, :, 3:5, :], times(one, 2), dst[:, :, 0:2, :],
                                                    ALU.subtract), s_split)
            pool.wait(mid)
            full_free[s] = q_nat_ready[slot] = pool.do(lambda e: e.tensor_tensor(
                dst[:, :, 5, :], left, dst[:, :, 3, :], ALU.subtract), s_split)

        def v_tasks(layer, b, col, slot, after=None):
            w = wv1 if layer else wv0
            tasks = []
            if layer:
                def ones_task():
                    pool.wait(v_read[slot])
                    pool.wait(valid_t)
                    pool.wait(v_const)
                    ones = pool.do(lambda e: e.tensor_copy(
                        v_sb[0:TT, slot, :, HD:8 * VW:VW],
                        valid[:, b, :].rearrange("p (i o) -> p i o", o=1).broadcast_to([TT, NT, 8])), s_ones)
                    v_ones[slot] = ones
                tasks.append(ones_task)
            for i in range(NT):
                t0, tn = tile(i)
                c = i // CT
                box = {}
                for k in range(KT):
                    def task(i=i, k=k, t0=t0, tn=tn, c=c, box=box):
                        mark = product(box, ctx_sb[:, k, t0:t0 + tn], w[:, k, col * P:(col + 1) * P], tn, P, k,
                                       (ctx_loaded[c], w_loaded["wv1"] if layer else w_ready["wv0"]))
                        if k == KT - 1:
                            ctx_read[c] = mark

                            def reader():
                                act.wait(mark)
                                act.wait(v_read[slot])
                                act.wait(v_const)
                                dst = v_sb[0:tn, slot, i, 0:8 * VW].rearrange("p (h e) -> p h e", e=VW)
                                src = box["bank"][0:tn, 0:P].rearrange("p (h d) -> p h d", d=HD)
                                if layer:
                                    act.wait(valid_t)
                                    make = lambda e: e.activation(dst[:, :, 0:HD], src, ACT.Copy,
                                                                  scale=valid[0:tn, b, i:i + 1])
                                else:
                                    make = lambda e: e.activation(dst[:, :, 0:HD], src, ACT.Copy)
                                work_free[box["i"]] = v_ready[slot] = act.do(make, s_act)
                            later.append((box["i"], reader))
                            if after is not None and (i % CT == CT - 1 or i == NT - 1):
                                load_ctx(after, c)
                    tasks.append(task)
            return tasks

        v_ones = [v_const, v_const]
        x_ready = [None] * (B * QT)

        def turn_x_tasks(b):
            tasks = []
            for q in range(QT):
                def task(q=q):
                    i, bank = work()
                    pe.wait(x_ready[b * QT + q])
                    for k in range(KT):
                        mark = pe.do(lambda e, k=k: e.transpose(
                            bank[:, k * P:(k + 1) * P], x_sb[:, b * QT + q, k * P:(k + 1) * P], ident[:, :]),
                            s_work if k == KT - 1 else None)

                    def reader():
                        act.wait(mark)
                        act.wait(xt_read[b % 2])
                        work_free[i] = xt_ready[b % 2] = act.do(lambda e: e.activation(
                            xt_sb[:, b % 2, :, q * P:(q + 1) * P],
                            bank[:, :].rearrange("p (k s) -> p k s", k=KT), ACT.Copy), s_act)
                    later.append((i, reader))
                tasks.append(task)
            return tasks

        k_slot_ready = [None] * 3
        k_slot_read = [None] * 3
        q_slot_ready = [None] * 3
        q_slot_read = [None] * 3
        q_unit = [None] * 3
        m_slot_ready = [None] * 3
        m_unit = [None] * 3

        def k_place(u):
            if u < L0:
                return (u // 4) % 3, u % 4
            return (L0 // 4 + u - L0) % 3, 0

        def stack(u):
            g, _ = k_place(u)
            if u < L0 and u % 4:
                return
            group, half = (u // 2, u % 2) if u >= L0 else (u // UB, u // 4 % 2)
            group, half = group % 2, half * 4 * HD
            for mark in k_dram_ready[group]:
                sp.wait(mark)
            for mark in k_slot_read[g] or ():
                sp.wait(mark)
            for r, part in enumerate(KPARTS):
                mark = load(k_stack[r * HD:(r + 1) * HD, 4 * g:4 * g + 4, :],
                            k_dram[group, part, half:half + 4 * HD, :].rearrange("(h d) t -> d h t", h=4),
                            s_kst[g])
            if u >= L0:
                b = (u - L0) // UB
                sp.wait(masks["neg"])
                sp.wait(stack_ones[g])
                mark = load(k_stack[MROW:KMAX, 4 * g:4 * g + 4, :],
                            neg_row[b:b + 1, :].rearrange("o (a t) -> o a t", a=1).broadcast_to([1, 4, T]),
                            s_kst[g])
            k_dram_read[group] = k_dram_read[group][-1:] + [mark]
            k_slot_ready[g] = mark

        def turn_q(u):
            i, bank16 = work16()
            s, slot = u % 3, u // 2 % 2
            pe.wait(q_nat_ready[slot])
            pe.wait(ident16_done)
            for h in range(GH):
                for q in range(QT):
                    last = h == GH - 1 and q == QT - 1
                    mark = pe.do(lambda e, h=h, q=q: e.transpose(
                        bank16[0:MROW, (h * QT + q) * P:(h * QT + q + 1) * P],
                        q_nat[:, slot, q * 8 + GH * (u % 2) + h, :], ident16[:, :]), s_work if last else None)
            q_nat_read[slot] = mark

            def reader():
                dve.wait(mark)
                for m in q_slot_read[s] or ():
                    dve.wait(m)
                work_free[i] = q_slot_ready[s] = dve.do(lambda e: e.tensor_copy(
                    q_stack[0:MROW, s, :, :].rearrange("d h q -> d (h q)"), bank16[0:MROW, :]), s_dve)
                q_unit[s] = u
            later.append((i, reader))

        max_free = [None] * 3
        m_nat_read = [None, None]
        max_done = [None] * 3
        max_turn = [0]

        def max_chunk():
            n = max_turn[0]
            u, at = n // CHUNKS, n % CHUNKS
            if u >= UNITS:
                return
            max_turn[0] += 1
            row, c = at // NM, at % NM
            h, q = row // QT, row % QT
            g, first = k_place(u)
            head = 4 * g + (first if u < L0 else h)
            lo, hi = c * MW, min(T, (c + 1) * MW)
            pe.wait(max_free[n % 3])
            pe.wait(k_slot_ready[g])
            pe.wait(stack_ones[g])
            pe.wait(q_slot_ready[u % 3])
            assert q_unit[u % 3] == u
            bank = max_bank[n % 3]
            mark = pe.do(lambda e: e.matmul(bank[:, 0:hi - lo], q_stack[0:KMAX, u % 3, h, q * P:(q + 1) * P],
                                            k_stack[0:KMAX, head, lo:hi], start=True, stop=True), s_rows)
            dve.wait(mark)
            max_free[n % 3] = dve.do(lambda e: e.tensor_reduce(
                chunk_max[:, u % 2, row, c:c + 1], bank[:, 0:hi - lo], AX.X, ALU.max), s_chunk)
            if at == CHUNKS - 1:
                max_done[u % 3] = mark
                dve.wait(max_free[n % 3])
                dve.wait(m_nat_read[u % 2])
                neg = dve.do(lambda e: e.tensor_reduce(neg_max[:, u % 2, :], chunk_max[:, u % 2, :, :], AX.X,
                                                       ALU.max, negate=True), s_dve)
                dve.wait(neg)
                dve.wait(m_const)
                high = dve.do(lambda e: e.tensor_copy(m_nat[:, u % 2, :, 1], neg_max[:, u % 2, :]), s_dve)
                dve.wait(high)
                low = dve.do(lambda e: e.tensor_tensor(m_nat[:, u % 2, :, 2], neg_max[:, u % 2, :],
                                                       m_nat[:, u % 2, :, 1], ALU.subtract), s_dve)
                turns.append((step_now[0], lambda: max_rows(u, low)))

        step_now = [0]
        turns = []

        def turn_all(now=0):
            while turns and not filling[0] and turns[0][0] < now:
                turns.pop(0)[1]()

        def max_rows(u, low):
            i, bank16 = work16()
            pe.wait(low)
            for row in range(ROWS):
                mark = pe.do(lambda e, row=row: e.transpose(
                    bank16[MROW:MROW + 32, row * P:(row + 1) * P], m_nat[:, u % 2, row, :], ident16[:, :],
                    tile_position=(0, MROW)), s_work if row == ROWS - 1 else None)
            m_nat_read[u % 2] = mark
            s = u % 3

            def reader():
                dve.wait(mark)
                for m in q_slot_read[s] or ():
                    dve.wait(m)
                dve.wait(max_done[s])
                work_free[i] = m_slot_ready[s] = dve.do(lambda e: e.tensor_copy(
                    q_stack[MROW:KEXP, s, :, :].rearrange("d h q -> d (h q)"), bank16[MROW:KEXP, :]), s_dve)
                m_unit[s] = u
            later.append((i, reader))

        score_free = [None] * 3
        half_turn = [0]
        value_free = [None]
        exp_done = {}

        def scores(u, i, half):
            n = half_turn[0]
            half_turn[0] += 1
            t0, tn = tile(i)
            g, first = k_place(u)
            s = u % 3
            bank, place = score_bank[n % 2], n % PLACES
            assert m_unit[s] == u, (u, i, m_unit, max_turn, len(turns), len(later))
            pe.wait(score_free[n % 2])
            pe.wait(k_slot_ready[g])
            pe.wait(q_slot_ready[s])
            pe.wait(m_slot_ready[s])
            if u < L0:
                mark = pe.do(lambda e: e.matmul(
                    bank[0:tn, :], k_stack[0:KEXP, 4 * g + first, t0:t0 + tn],
                    q_stack[0:KEXP, s, 2 * half:2 * half + 2, :].rearrange("p h q -> p (h q)"),
                    start=True, stop=True), s_scores)
            else:
                for j in range(2):
                    h = 2 * half + j
                    mark = pe.do(lambda e, j=j, h=h: e.matmul(
                        bank[0:tn, j * S:(j + 1) * S], k_stack[0:KEXP, 4 * g + h, t0:t0 + tn],
                        q_stack[0:KEXP, s, h, :], start=True, stop=True), s_scores if j else None)
            if i == NT - 1 and half == 1:
                q_slot_read[s] = (mark,)
                if u >= L0 or u % 4 == 3:
                    k_slot_read[g] = (mark, )
            act.wait(mark)
            act.wait(p_free[place])
            score_free[n % 2] = act.do(lambda e: e.activation(
                p_sb[0:tn, place, :], bank[0:tn, :], ACT.Exp, scale=SCALE), s_exp)
            exp_done[u, i, half] = score_free[n % 2], place

        def values(u, i):
            t0, tn = tile(i)
            slot = (u // UB) % 2 if u < L0 else ((u - L0) // 2) % 2
            if i == 0:
                pe.wait(value_free[0])
                pe.wait(v_ready[slot])
                pe.wait(v_ones[slot])
            places = []
            for half in range(2):
                mark, place = exp_done.pop((u, i, half))
                pe.wait(mark)
                places.append(place)
            for j in range(GH):
                head = u % UB if u < L0 else 4 * (u % 2) + j
                done = pe.do(lambda e, j=j, head=head: e.matmul(
                    value_bank[32 * j:32 * j + 32, 0:S], v_sb[0:tn, slot, i, head * VW:head * VW + 32],
                    p_sb[0:tn, places[j // 2], j % 2 * S:(j % 2 + 1) * S], start=(i == 0),
                    stop=(i == NT - 1)), s_value if j == GH - 1 else None)
            for place in places:
                p_free[place] = done
            if i == NT - 1:
                v_read[slot] = done
                finish(u, done)

        o_read = [None, None]
        recip_turn = [0]
        att_ready = [None]
        att_unit = [None]
        att_read = [None]

        def finish(u, done):
            s = u % 2
            dve.wait(done)
            dve.wait(o_read[s])
            value_free[0] = dve.do(lambda e: e.tensor_copy(o_sb[:, s, :], value_bank[:, 0:S]), s_dve)
            copied = value_free[0]
            h0 = GH * (u % UB)

            def turn():
                i, bank = work()
                pe.wait(copied)
                for q in range(QT):
                    mark = pe.do(lambda e, q=q: e.transpose(bank[:, q * P:(q + 1) * P],
                                                            o_sb[:, s, q * P:(q + 1) * P], ident[:, :]), s_work)
                o_read[s] = mark
                view = bank[:, 0:QT * P].rearrange("p (q h e) -> p q h e", q=QT, h=GH)

                def reader():
                    dve.wait(mark)
                    dve.wait(att_read[0])
                    inv = dve.do(lambda e: e.reciprocal(recip[:, s, :, :], view[:, :, :, HD]), s_dve)
                    dve.wait(inv)
                    for q in range(QT):
                        m = dve.do(lambda e, q=q: e.tensor_tensor(
                            att[:, q, h0 * HD:(h0 + GH) * HD].rearrange("p (h d) -> p h d", h=GH),
                            view[:, q, :, 0:HD],
                            recip[:, s, q, :].rearrange("p (h o) -> p h o", o=1).broadcast_to([P, GH, HD]),
                            ALU.mult), s_dve)
                    work_free[i] = att_ready[0] = m
                    att_unit[0] = u
                later.append((i, reader))
            turns.append((step_now[0], turn))

        att_t_ready = [None] * QT
        att_t_read = [None]

        def out_tasks(layer, b):
            tasks = []
            ready = [None]

            def first():
                ready[0] = att_ready[0]
                if layer:
                    dve.wait(att_ready[0])
                    dve.wait(w_loaded["rows"])
                    for q in range(QT):
                        ready[0] = dve.do(lambda e, q=q: e.tensor_tensor(
                            att[:, q, :], att[:, q, :], row_bias[:, 0, :], ALU.add), s_dve)
            tasks.append(first)
            for q in range(QT):
                def task(q=q):
                    i, bank = work()
                    pe.wait(ready[0])
                    for k in range(KT):
                        mark = pe.do(lambda e, k=k: e.transpose(
                            bank[:, k * P:(k + 1) * P], att[:, q, k * P:(k + 1) * P], ident[:, :]),
                            s_work if k == KT - 1 else None)
                    att_read[0] = mark

                    def reader():
                        act.wait(mark)
                        act.wait(att_t_read[0])
                        work_free[i] = att_t_ready[q] = act.do(lambda e: e.activation(
                            att_t[:, :, q * P:(q + 1) * P], bank[:, :].rearrange("p (k s) -> p k s", k=KT),
                            ACT.Copy), s_act)
                    later.append((i, reader))
                tasks.append(task)
            for q in range(QT):
                box = {}
                for k in range(KT):
                    def task(q=q, k=k, box=box):
                        mark = product(box, att_t[:, k, q * P:(q + 1) * P], wo[:, k, :], P, H, k,
                                       (att_t_ready[q], w_loaded["wo1"] if layer else w_ready["wo"]))
                        if k < KT - 1:
                            return
                        wo_read[0] = mark
                        if q == QT - 1:
                            att_t_read[0] = mark
                        later.append((box["i"], lambda: (norm if layer else add)(b, q, mark, box)))
                    tasks.append(task)
            return tasks

        wo_read = [None]

        def add(b, q, mark, box):
            row, bank = b * QT + q, box["bank"]
            dve.wait(mark)
            dve.wait(x_loaded)
            work_free[box["i"]] = x_ready[row] = dve.do(lambda e: e.tensor_tensor(
                x_sb[:, row, :], bank[:, :], x_sb[:, row, :], ALU.add), s_dve)

        slow = []

        def step_norm():
            if slow:
                slow.pop(0)()

        def norm(b, q, mark, box):
            row, bank = b * QT + q, box["bank"]
            y = x_sb[:, row, :]
            dve.wait(mark)
            dve.wait(x_ready[row])
            work_free[box["i"]] = added = dve.do(lambda e: e.tensor_tensor(y, bank[:, :], y, ALU.add), s_dve)

            def biased():
                dve.wait(added)
                done = dve.do(lambda e: e.tensor_tensor(y, y, row_bias[:, 1, :], ALU.add), s_dve)
                dve.wait(done)
                done = dve.do(lambda e: e.bn_stats(stats[:, q, :], y), s_dve)
                dve.wait(done)
                norm_ready[q] = dve.do(lambda e: e.bn_aggr(moments[:, q, :], stats[:, q, :]), s_dve)
            slow.append(biased)
            if q < QT - 1:
                return

            def variance():
                dve.wait(norm_ready[QT - 1])
                norm_ready[0] = dve.do(lambda e: e.tensor_scalar(rstd[:, :], moments[:, :, 1], EPS, None,
                                                                 ALU.add), s_dve)

            def root():
                act.wait(norm_ready[0])
                norm_ready[0] = act.do(lambda e: e.activation(rstd[:, :], rstd[:, :], ACT.Sqrt), s_act)

            def inverse():
                dve.wait(norm_ready[0])
                norm_ready[0] = dve.do(lambda e: e.reciprocal(rstd[:, :], rstd[:, :]), s_dve)
            slow.extend((variance, root, inverse))
            for r in range(QT):
                slow.append(lambda r=r: normalise(b, r))

        norm_ready = [None] * QT

        def normalise(b, q):
            y = x_sb[:, b * QT + q, :]
            dve.wait(norm_ready[0])
            done = dve.do(lambda e: e.tensor_scalar(y, y, moments[:, q, 0:1], rstd[:, q:q + 1], ALU.subtract,
                                                    ALU.mult), s_dve)
            pool.wait(done)
            pool.wait((s_split, s_split.value))
            done = pool.do(lambda e: e.tensor_tensor(y, y, row_bias[:, 2, :], ALU.mult), s_split)
            pool.wait(done)
            done = pool.do(lambda e: e.tensor_tensor(y, y, row_bias[:, 3, :], ALU.add), s_split)
            sp.wait(done)
            load(out[b, q * P:(q + 1) * P, :], y, s_out)

        def run(tasks):
            for t in tasks:
                t()
            flush()

        fold_lora("k")
        load_lora("v")
        first_k = k_tasks(0, 0, 0)
        run(first_k[:KT])
        fold_lora("q")
        load_w("wo", wo, w0["Wo"])
        load_lora("o")
        run(q_tasks(0, 0, 0))
        constant_rows(0, dve, s_dve)
        run(first_k[KT:])
        stack(0)
        run(q_tasks(0, 0, 1))
        turn_q(0)
        turn_q(1)
        flush()
        for g in (1, 2):
            constant_rows(g, pool, s_split)
        fold_lora("v")
        read_mask()
        valid_t = turn_mask()
        load_w("wk1", wk1, w1["Wk"])
        load_w("wv1", wv1, w1["Wv"])
        x_loaded = load(x_sb[:, :, :], x.rearrange("b (q p) h -> p (b q) h", p=P), s_w["x"])
        for n, v in enumerate(("bv", "bo", "ln_g", "ln_b", "bq")):
            w_loaded["rows"] = load(row_bias[:, n, :], w1[v].rearrange("(o n) -> o n", o=1)
                                    .broadcast_to([P, H]), s_w["rows"])
        w_loaded["cols"] = load(col_bias[:, :], w1["bk"], s_w["cols"])
        v0 = v_tasks(0, 0, 0, 0)
        AHEAD = 4 * KT
        assert len(v0) <= AHEAD + CHUNKS + LEAD
        run(v0[:AHEAD])
        for n in range(CHUNKS + LEAD):
            max_chunk()
            if AHEAD + n < len(v0):
                v0[AHEAD + n]()
            turn_all(1)
        flush()
        fold_lora("o")
        flush()

        def after_value(u):
            tasks = []
            if u % UB == 0 and u > 0:
                b = u // UB - 1
                tasks += out_tasks(b // B, b % B)
            v = u + 2
            if v % 2 == 0 and L0 <= v < UNITS:
                b = (v - L0) // UB
                last = v % UB == UB - 2 and b + 1 < B
                own = v_tasks(1, b, v % UB // 2, v // 2 % 2, b + 1 if last else None)
                tasks = tasks[:1] + own[:1 + 2 * KT] + tasks[1:] + own[1 + 2 * KT:]
            return tasks

        def window(u):
            tasks = []
            if u == L0 + 1:
                def task():
                    sp.wait(wo_read[0])
                    load_w("wo1", wo, w1["Wo"])
                tasks.append(task)
            if u < L0 - UB:
                b = u // UB + 1
                at = u % UB
                vt, kt = v_tasks(0, b, 0, b % 2), k_tasks(0, 0, b)
                if at == 0:
                    for c in range(NC):
                        tasks.append(lambda c=c: load_ctx(b, c))
                    tasks.append(lambda: load_xt(b))
                if at < 3:
                    n = KT * -(-len(vt) // (3 * KT))
                    tasks += v_rest.setdefault(b, vt)[at * n:(at + 1) * n]
                elif at < 6:
                    n = KT * -(-len(kt) // (3 * KT))
                    tasks += k_rest.setdefault(b, kt)[(at - 3) * n:(at - 2) * n]
            if u == L0 - 6:
                for c in range(NC):
                    tasks.append(lambda c=c: load_ctx(0, c))
            v = u + 3
            if v % 2 == 0 and 4 <= v < UNITS:
                layer, b = v // L0, v % L0 // UB
                if layer:
                    tasks += k_tasks(1, v % UB // 2, v // 2)
                tasks += q_tasks(layer, b, v // 2)
                if v == L0 - 2:
                    def task():
                        sp.wait(xt_read[(B - 1) % 2])
                        load_w("wq1", wq, w1["Wq"])
                    tasks.append(task)
            if u + 4 >= L0 and (u + 4) % UB == 0 and u + 4 < UNITS:
                tasks += turn_x_tasks((u + 4 - L0) // UB)
            return tasks

        v_rest, k_rest = {}, {}
        waiting = []
        for u in range(UNITS):
            if u + 2 < UNITS:
                stack(u + 2)
            tasks = window(u)
            ran = 0
            base = max_turn[0]
            for i in range(NT):
                if i in (LAG, LAG + 2):
                    while filling[0]:
                        tasks[ran]()
                        ran += 1
                    if i == LAG and u + 2 < UNITS:
                        turn_q(u + 2)
                    if i == LAG + 2:
                        assert not u or att_unit[0] == u - 1
                        tasks[ran:ran] = after_value(u)
                goal = base + CHUNKS * (i + 1) // NT
                scores(u, i, 0)
                if max_turn[0] < goal:
                    max_chunk()
                scores(u, i, 1)
                upto = max(ran, ran + (len(tasks) - ran) // (NT - i))
                mid = (ran + upto + 1) // 2
                while ran < mid:
                    tasks[ran]()
                    ran += 1
                    turn_all(step_now[0])
                if max_turn[0] < goal and max_turn[0] < UNITS * CHUNKS:
                    max_chunk()
                waiting.append((u, i))
                if len(waiting) > LAG:
                    values(*waiting.pop(0))
                while ran < upto:
                    tasks[ran]()
                    ran += 1
                    turn_all(step_now[0])
                while max_turn[0] < goal and max_turn[0] < UNITS * CHUNKS:
                    max_chunk()
                while turns and turns[0][0] < step_now[0]:
                    if filling[0]:
                        tasks[ran]()
                        ran += 1
                    turn_all(step_now[0])
                step_now[0] += 1
                flush()
                step_norm()
        while waiting:
            values(*waiting.pop(0))
        turn_all(step_now[0] + 1)
        flush()
        run(out_tasks(1, B - 1))
        while slow:
            step_norm()
        for s in s_kdw:
            sp.wait((s, s.value))
        sp.wait((s_out, s_out.value))

        block = ctx.enter_context(nc.Block())
        block.sync(lambda e: sp.play(e))
        block.tensor(lambda e: pe.play(e))
        block.scalar(lambda e: act.play(e))
        block.vector(lambda e: dve.play(e))
        block.gpsimd(lambda e: pool.play(e))


def kernel(**inputs):
    import numpy as np
    import concourse.bacc as bacc
    from concourse.bass_utils import run_bass_kernel_spmd

    a = {k: np.asarray(v) for k, v in inputs.items()}
    H = a["x"].shape[2]
    arrays = {
        "x": a["x"],
        "xT": a["x"].transpose(0, 2, 1),
        "ctxT": a["ctx_4096"].transpose(0, 2, 1),
        "mask": a["mask_BxS2_ik0"],
    }
    for n in "qkvo":
        arrays[f"l0_W{n}"] = a[f"L0_xattn_W{n}"]
        arrays[f"l0_A{n}T"] = a[f"L0_xattn_A{n}"].T
        arrays[f"l0_B{n}"] = a[f"L0_xattn_B{n}"]
        arrays[f"l1_W{n}"] = a[f"L1_xattn_W{n}"].T
    arrays["l1_bk"] = a["L1_xattn_bk"].reshape(H // 128, 128).T
    for n in ("bq", "bv", "bo", "ln_g", "ln_b"):
        arrays[f"l1_{n}"] = a[f"L1_xattn_{n}"]
    arrays = {k: np.ascontiguousarray(v) for k, v in arrays.items()}

    nc = bacc.Bacc("TRN2", target_bir_lowering=False, num_devices=1)
    t = {k: nc.dram_tensor(k, v.shape, mybir.dt.from_np(v.dtype), kind="ExternalInput").ap()
         for k, v in arrays.items()}
    out = nc.dram_tensor("out", a["x"].shape, F32, kind="ExternalOutput").ap()
    w0 = {k[3:]: v for k, v in t.items() if k.startswith("l0_")}
    w1 = {k[3:]: v for k, v in t.items() if k.startswith("l1_")}
    cross_attention_pair(nc, t["x"], t["xT"], t["ctxT"], t["mask"], w0, w1, out)
    return run_bass_kernel_spmd(nc, [arrays], core_ids=[0]).results[0]["out"]
```
